# Optimizing a Trainium2 kernel written in Bass

```python
import numpy as np
import jax
import jax.numpy as jnp

def _softmax(x, axis=-1):
    return jax.nn.softmax(x, axis=axis)

def _gelu(x):
    return jax.nn.gelu(x, approximate=True)

def _silu(x):
    return jax.nn.silu(x)

def _sigmoid(x):
    return jax.nn.sigmoid(x)

def _layernorm(x, axis=-1, eps=1e-05):
    m = jnp.mean(x, axis=axis, keepdims=True)
    v = jnp.var(x, axis=axis, keepdims=True)
    return (x - m) / jnp.sqrt(v + eps)

def _scatter_add(tgt, idx, src, axis=0):
    return tgt.at[idx].add(src)

def _segment_sum(src, seg, n):
    return jax.ops.segment_sum(src, seg, n)
kernel_name = 'mk_cond_resid_d1_seqx_r4_d7d879'

def setup_inputs(seed: int=0):
    np.random.seed(seed)
    _w = jnp.asarray

    def _rec_inputs():
        import jax
        import jax.numpy as jnp
        _rk = jax.random.key(seed)
        x = -0.0005207 + 1.001 * jax.random.normal(jax.random.fold_in(_rk, 1), (16, 256, 256), jnp.float32)
        _lenS = 256 - jax.random.randint(jax.random.fold_in(_rk, 7), (16,), 0, max(1, 256 // 4) + 1, jnp.int32)
        _lenS2 = 256 - jax.random.randint(jax.random.fold_in(_rk, 8), (16,), 0, max(1, 256 // 4) + 1, jnp.int32)
        fside_Bx8_0 = jax.random.uniform(jax.random.fold_in(_rk, 11), (16, 8), jnp.float32, 0.0, 0.556406)
        condB_sharedgateprob = jax.random.uniform(jax.random.fold_in(_rk, 12), (16,), jnp.float32, 0.0, 0.794948)
        return (x, fside_Bx8_0, condB_sharedgateprob)
    x, fside_Bx8_0, condB_sharedgateprob = _rec_inputs()

    def _L0_cond_setup():
        import jax, jax.numpy as jnp
        import numpy as np
        E, B, S, D, F = (8, 2, 256, 256, 1024)
        key = jax.random.key(seed)
        ks = jax.random.split(key, 9)
        sc_d = 1.0 / np.sqrt(D)
        sc_f = 1.0 / np.sqrt(F)
        hidden_states = jax.random.normal(ks[0], (B, S, D), dtype=jnp.float32)
        gating_probs = jax.nn.softmax(jax.random.normal(ks[1], (B, E), dtype=jnp.float32), axis=-1)
        shared_gate_prob = jax.nn.sigmoid(jax.random.normal(ks[2], (B, 1), dtype=jnp.float32))
        Wg = jax.random.normal(ks[3], (E, D, F), dtype=jnp.float32) * sc_d
        Wu = jax.random.normal(ks[4], (E, D, F), dtype=jnp.float32) * sc_d
        Wd = jax.random.normal(ks[5], (E, F, D), dtype=jnp.float32) * sc_f
        Sg = jax.random.normal(ks[6], (D, F), dtype=jnp.float32) * sc_d
        Su = jax.random.normal(ks[7], (D, F), dtype=jnp.float32) * sc_d
        Sd = jax.random.normal(ks[8], (F, D), dtype=jnp.float32) * sc_f
        return {'hidden_states': hidden_states, 'gating_probs': gating_probs, 'shared_gate_prob': shared_gate_prob, 'Wg': Wg, 'Wu': Wu, 'Wd': Wd, 'Sg': Sg, 'Su': Su, 'Sd': Sd}
    _L0_cond_all = _L0_cond_setup()
    _L0_cond_in = {k: v for k, v in _L0_cond_all.items() if k in ('Wg', 'Wu', 'Wd', 'Sg', 'Su', 'Sd')}
    del _L0_cond_all
    return {'x': x, 'fside_Bx8_0': fside_Bx8_0, 'condB_sharedgateprob': condB_sharedgateprob, 'L0_cond_Wg': _L0_cond_in['Wg'], 'L0_cond_Wu': _L0_cond_in['Wu'], 'L0_cond_Wd': _L0_cond_in['Wd'], 'L0_cond_Sg': _L0_cond_in['Sg'], 'L0_cond_Su': _L0_cond_in['Su'], 'L0_cond_Sd': _L0_cond_in['Sd']}

def reference(x, fside_Bx8_0, condB_sharedgateprob, L0_cond_Wg, L0_cond_Wu, L0_cond_Wd, L0_cond_Sg, L0_cond_Su, L0_cond_Sd):
    import jax
    import jax.numpy as jnp

    def _L0_cond_ref(hidden_states, gating_probs, shared_gate_prob, Wg, Wu, Wd, Sg, Su, Sd):
        import jax, jax.numpy as jnp
        import numpy as np
        E, B, S, D, F = (8, 2, 256, 256, 1024)
        h = hidden_states
        g = jnp.einsum('bsd,edf->ebsf', h, Wg)
        u = jnp.einsum('bsd,edf->ebsf', h, Wu)
        expert_outs = jnp.einsum('ebsf,efd->ebsd', jax.nn.silu(g) * u, Wd)
        expert_output = jnp.einsum('be,ebsd->bsd', gating_probs, expert_outs)
        shared = jnp.einsum('bsf,fd->bsd', jax.nn.silu(h @ Sg) * (h @ Su), Sd)
        sg = shared_gate_prob[:, :, None]
        return (1.0 - sg) * expert_output + sg * shared
    x = x + _L0_cond_ref(x, fside_Bx8_0, condB_sharedgateprob[:, None], L0_cond_Wg, L0_cond_Wu, L0_cond_Wd, L0_cond_Sg, L0_cond_Su, L0_cond_Sd)
    return x

_drawn_inputs = setup_inputs


def setup_inputs(seed=0):
    import zlib

    import numpy as np

    out = dict(_drawn_inputs(seed))
    spreads = {}
    factors = {}
    for name, (base, spread) in spreads.items():
        noise = np.random.default_rng([zlib.crc32(name.encode()), seed]).standard_normal(out[name].shape)
        drawn = base * np.exp(spread * noise) if base else spread * noise
        out[name] = jnp.asarray(drawn.astype(out[name].dtype))
    for name, factor in factors.items():
        out[name] = (out[name] * factor).astype(out[name].dtype)
    return out
```

```python
from contextlib import ExitStack

import concourse.bass as bass
from concourse import mybir

F32 = mybir.dt.float32
F32R = mybir.dt.float32r
ALU = mybir.AluOpType
ACT = mybir.ActivationFunctionType

P = 128
TOKENS = 512
S_BUFS = 2
H_BUFS = 4


def moe_kernel(nc, xT, w, probs, shared_gate, out):
    TILES, _, DC, _ = xT.shape
    EXPERTS, CHUNKS, _, W_COLS = w.shape
    BATCH, ROUTED = probs.shape
    D = DC * P
    HALVES = BATCH // TILES
    SEQ = TOKENS // HALVES
    assert EXPERTS == ROUTED + 1 and W_COLS == 3 * D and TILES % 2 == 0 and HALVES * TILES == BATCH
    UNITS = TILES * CHUNKS
    PAIRS = (TILES - 2) // 2
    FREED = 2
    LEAD = 3
    GATE = slice(0, D)
    REST = slice(D, 3 * D)

    with ExitStack() as ctx:

        def sb(name, shape, dt=F32):
            return ctx.enter_context(nc.sbuf_tensor(name, shape, dt))

        def sem(name):
            return ctx.enter_context(nc.semaphore(name))

        acc = sb("acc", [P, TILES, DC, TOKENS])
        x_hi = sb("x_hi", [P, TILES, DC, TOKENS], F32R)
        x_lo = sb("x_lo", [P, TILES, DC, TOKENS], F32R)
        w_raw = sb("w_raw", [P, CHUNKS, W_COLS])
        w_hi = sb("w_hi", [P, CHUNKS, W_COLS], F32R)
        w_lo = sb("w_lo", [P, CHUNKS, W_COLS], F32R)
        silu = sb("silu", [P, S_BUFS, TOKENS])
        h = sb("h", [P, S_BUFS, TOKENS])
        h_hi = sb("h_hi", [P, H_BUFS, TOKENS], F32R)
        h_lo = sb("h_lo", [P, H_BUFS, TOKENS], F32R)
        probs_sb = sb("probs_sb", [P, BATCH, ROUTED])
        shared_sb = sb("shared_sb", [P, BATCH])
        routed_part = sb("routed_part", [P, BATCH])
        coef = sb("coef", [P, EXPERTS * BATCH])
        warm = sb("warm", [P, 1])

        gate_ps = ctx.enter_context(nc.psum_tensor("gate_ps", [P, 2, TOKENS], F32))
        up_ps = ctx.enter_context(nc.psum_tensor("up_ps", [P, 2, TOKENS], F32))
        down_ps = ctx.enter_context(nc.psum_tensor("down_ps", [P, 2, DC, TOKENS], F32))

        w0_gate_loaded = sem("w0_gate_loaded")
        x0_loaded = [sem(f"x0_loaded{c}") for c in range(DC)]
        w_loaded = [sem(f"w_loaded{k}") for k in range(CHUNKS)]
        x_loaded = [sem(f"x_loaded{t}") for t in range(1, TILES)]
        gates_loaded = sem("gates_loaded")
        stored = sem("stored")
        w_hi_done = sem("w_hi_done")
        w_split = sem("w_split")
        w0_gate_hi_done = sem("w0_gate_hi_done")
        w0_gate_split = sem("w0_gate_split")
        x0_hi_done = [sem(f"x0_hi_done{c}") for c in range(DC)]
        x0_split = sem("x0_split")
        x_hi_done = sem("x_hi_done")
        x_split = sem("x_split")
        gate_done = sem("gate_done")
        up_done = sem("up_done")
        down_done = sem("down_done")
        silu_done = sem("silu_done")
        prod_done = sem("prod_done")
        h_hi_done = sem("h_hi_done")
        h_split = sem("h_split")
        tile_added = sem("tile_added")
        last_sums = sem("last_sums")
        last_added = sem("last_added")
        coef_steps = sem("coef_steps")
        warm_set = sem("warm_set")
        warmed = sem("warmed")

        block = ctx.enter_context(nc.Block())

        @block.sync
        def _(sp):
            def load_weights(e, k):
                sp.dma_start(w_raw[:, k, :], w[e, k]).then_inc(w_loaded[k], 16)

            def load_tokens(t):
                sp.dma_start(acc[:, t], xT[t]).then_inc(x_loaded[t - 1], 16)

            sp.dma_start(acc[:, 0, 0, :], xT[0, :, 0, :]).then_inc(x0_loaded[0], 16)
            sp.dma_start(w_raw[:, 0, GATE], w[0, 0, :, GATE]).then_inc(w0_gate_loaded, 16)
            for c in range(1, DC):
                sp.dma_start(acc[:, 0, c, :], xT[0, :, c, :]).then_inc(x0_loaded[c], 16)
            sp.dma_start(w_raw[:, 0, REST], w[0, 0, :, REST]).then_inc(w_loaded[0], 16)
            for k in range(1, CHUNKS):
                load_weights(0, k)
            for t in range(1, TILES):
                load_tokens(t)
            with sp.Fori(1, EXPERTS) as e:
                for k in range(CHUNKS):
                    sp.wait_ge(w_split, (e - 1) * CHUNKS + k + 1)
                    sp.dma_start(
                        w_raw[:, k, :], w[bass.ds(e, 1), k, :, :].rearrange("a p c -> (a p) c")
                    ).then_inc(w_loaded[k], 16)
            with sp.Fori(0, TILES - 1) as t:
                sp.wait_ge(tile_added, (EXPERTS - 1) * TILES + 1 + t)
                sp.dma_start(
                    out[bass.ds(t, 1)].rearrange("a p c n -> (a p) c n"),
                    acc[:, bass.ds(t, 1)].rearrange("p a c n -> p (a c) n"),
                ).then_inc(stored, 16)
            for c in range(DC):
                sp.wait_ge(last_added, c + 1)
                sp.dma_start(out[TILES - 1, :, c, :], acc[:, TILES - 1, c, :]).then_inc(stored, 16)
            sp.wait_ge(stored, 16 * (TILES - 1 + DC))

        @block.gpsimd
        def _(pool):
            pool.dma_start(probs_sb[:], probs.partition_broadcast(P)).then_inc(gates_loaded, 16)
            pool.dma_start(shared_sb[:], shared_gate.partition_broadcast(P)).then_inc(gates_loaded, 16)
            for t in range(1, TILES):
                pool.wait_ge(x_loaded[t - 1], 16)
                nc.gpsimd.tensor_copy(x_hi[:, t], acc[:, t]).then_inc(x_hi_done, 1)
                pool.wait_ge(x_hi_done, t)
                nc.gpsimd.tensor_tensor(
                    x_lo[:, t], acc[:, t], x_hi[:, t].bitcast(F32), ALU.subtract
                ).then_inc(x_split, 1)

        @block.tensor
        def _(pe):
            def product(out_ps, k, cols, moving_hi, moving_lo, start, stop):
                nc.tensor.matmul(out_ps, w_hi[:, k, cols], moving_hi, start=start, stop=False)
                nc.tensor.matmul(out_ps, w_hi[:, k, cols], moving_lo, start=False, stop=False)
                return nc.tensor.matmul(out_ps, w_lo[:, k, cols], moving_hi, start=False, stop=stop)

            def tile_x(t):
                if isinstance(t, int):
                    return [(x_hi[:, t, c, :], x_lo[:, t, c, :]) for c in range(DC)]
                return [
                    tuple(x[:, bass.ds(t, 1), c, :].rearrange("p a n -> p (a n)") for x in (x_hi, x_lo))
                    for c in range(DC)
                ]

            def first_gate():
                g = gate_ps[:, 0, :]
                for c in range(DC):
                    cols = slice(c * P, (c + 1) * P)
                    if c == 0:
                        pe.wait_ge(w0_gate_hi_done, 1)
                    pe.wait_ge(x0_hi_done[c], 1)
                    nc.tensor.matmul(g, w_hi[:, 0, cols], x_hi[:, 0, c, :], start=(c == 0), stop=False)
                    pe.wait_ge(x0_split, c + 1)
                    nc.tensor.matmul(g, w_hi[:, 0, cols], x_lo[:, 0, c, :], start=False, stop=False)
                pe.wait_ge(w0_gate_split, 1)
                for c in range(DC):
                    cols = slice(c * P, (c + 1) * P)
                    last = nc.tensor.matmul(g, w_lo[:, 0, cols], x_hi[:, 0, c, :], start=False, stop=(c == DC - 1))
                last.then_inc(gate_done, 1)

            def gate_up(e, T, k, x, wait_banks=True, only_up=False):
                pe.wait_ge(w_split, e * CHUNKS + k + 1)
                sides = ((gate_ps, 0, gate_done, silu_done), (up_ps, D, up_done, prod_done))
                for ps, column0, done, used in sides[1:] if only_up else sides:
                    if wait_banks:
                        pe.wait_ge(used, T * CHUNKS + k - 1)
                    for c in range(DC):
                        cols = slice(column0 + c * P, column0 + (c + 1) * P)
                        last = product(ps[:, k % 2, :], k, cols, *x[c], start=(c == 0), stop=(c == DC - 1))
                    last.then_inc(done, 1)

            def down(T, k, parity, very_last=False):
                pe.wait_ge(h_split, T * CHUNKS + k + 1)
                for c in range(DC):
                    cols = slice(2 * D + c * P, 2 * D + (c + 1) * P)
                    last = product(
                        down_ps[:, parity, c, :], k, cols, h_hi[:, k % H_BUFS, :], h_lo[:, k % H_BUFS, :],
                        start=(k == 0), stop=(k == CHUNKS - 1),
                    )
                    if very_last and c < DC - 1:
                        last.then_inc(last_sums, 1)
                last.then_inc(down_done, 1)

            def tile(e, T, parity, x, following, wait_x=None, wait_added=True, next_expert=None):
                for k in range(CHUNKS):
                    down(T, k, parity)
                    if k < CHUNKS - 2:
                        gate_up(e, T, k + 2, x)
                        continue
                    if k == CHUNKS - 2 and wait_x is not None:
                        pe.wait_ge(x_split, wait_x)
                    if k == CHUNKS - 2 and wait_added:
                        pe.wait_ge(tile_added, T)
                    gate_up(e if next_expert is None else next_expert, T + 1, k + 2 - CHUNKS, following)

            def last_tile(e, T, parity, x):
                for k in range(CHUNKS):
                    if k == CHUNKS - 3:
                        gate_up(e, T, CHUNKS - 1, x)
                    down(T, k, parity, very_last=(k == CHUNKS - 1))
                    if k < CHUNKS - 3:
                        gate_up(e, T, k + 2, x)

            def pairs_of(e):
                with pe.Fori(0, PAIRS) as q:
                    t = 2 * q + 1
                    T = e * TILES + t
                    xs = [tile_x(t), tile_x(t + 1), tile_x(t + 2)]
                    tile(e, T, 1, xs[0], xs[1], wait_x=t + 1)
                    tile(e, T + 1, 0, xs[1], xs[2], wait_x=t + 2)

            last_t = TILES - 1
            first_gate()
            gate_up(0, 0, 0, tile_x(0), wait_banks=False, only_up=True)
            gate_up(0, 0, 1, tile_x(0), wait_banks=False)
            tile(0, 0, 0, tile_x(0), tile_x(1), wait_x=1, wait_added=False)
            with pe.Fori(0, EXPERTS - 1) as e:
                pairs_of(e)
                tile(e, e * TILES + last_t, 1, tile_x(last_t), tile_x(0), next_expert=e + 1)
                tile(e + 1, (e + 1) * TILES, 0, tile_x(0), tile_x(1))
            pairs_of(EXPERTS - 1)
            last_tile(EXPERTS - 1, (EXPERTS - 1) * TILES + last_t, 1, tile_x(last_t))

        @block.scalar
        def _(act):
            def split_weights(e, k, down_unit=None):
                act.wait_ge(w_loaded[k], (e + 1) * 16)
                if down_unit is not None:
                    act.wait_ge(down_done, down_unit + 1)
                nc.scalar.copy(w_hi[:, k, :], w_raw[:, k, :]).then_inc(w_hi_done, 1)

            def unit(T, k, first=False):
                n = T * CHUNKS + k
                act.wait_ge(gate_done, n + 1)
                if not (first and k < S_BUFS):
                    act.wait_ge(prod_done, n + 1 - S_BUFS)
                nc.scalar.activation(silu[:, k % S_BUFS, :], gate_ps[:, k % 2, :], ACT.Silu).then_inc(silu_done, 1)
                act.wait_ge(prod_done, n + 1)
                if not (first and k < H_BUFS):
                    act.wait_ge(down_done, n + 1 - H_BUFS)
                nc.scalar.copy(h_hi[:, k % H_BUFS, :], h[:, k % S_BUFS, :]).then_inc(h_hi_done, 1)

            def tile(T, first=False, splits=None):
                for k in range(CHUNKS):
                    unit(T, k, first)
                    if splits is not None:
                        splits(k)

            def first_splits(k):
                if k + LEAD < CHUNKS:
                    split_weights(0, k + LEAD)

            def late_splits(e, T_last):

                def at(k):
                    c = k + CHUNKS - FREED
                    if c < CHUNKS:
                        split_weights(e, c, T_last * CHUNKS + c)

                return at

            def early_splits(e, T_last):

                def at(k):
                    c = k - FREED
                    if c >= 0:
                        split_weights(e, c, T_last * CHUNKS + c)

                return at

            def pairs_of(e):
                with act.Fori(0, PAIRS) as q:
                    T = e * TILES + 2 * q + 1
                    tile(T)
                    tile(T + 1)

            last_t = TILES - 1
            act.wait_ge(warm_set, 1)
            nc.scalar.activation(warm[:], warm[:], ACT.Silu).then_inc(warmed, 1)
            act.wait_ge(w0_gate_loaded, 16)
            nc.scalar.copy(w_hi[:, 0, GATE], w_raw[:, 0, GATE]).then_inc(w0_gate_hi_done, 1)
            for c in range(1, DC):
                act.wait_ge(x0_loaded[c], 16)
                nc.scalar.copy(x_hi[:, 0, c, :], acc[:, 0, c, :]).then_inc(x0_hi_done[c], 1)
            act.wait_ge(w_loaded[0], 16)
            nc.scalar.copy(w_hi[:, 0, REST], w_raw[:, 0, REST]).then_inc(w_hi_done, 1)
            for k in range(1, LEAD):
                split_weights(0, k)
            tile(0, first=True, splits=first_splits)
            with act.Fori(0, EXPERTS - 1) as e:
                pairs_of(e)
                T_last = e * TILES + last_t
                tile(T_last, splits=early_splits(e + 1, T_last))
                tile(T_last + 1, splits=late_splits(e + 1, T_last))
            pairs_of(EXPERTS - 1)
            tile((EXPERTS - 1) * TILES + last_t)

        @block.vector
        def _(dve):
            def split_weights(e, k):
                dve.wait_ge(w_hi_done, e * CHUNKS + k + 1)
                nc.vector.tensor_tensor(
                    w_lo[:, k, :], w_raw[:, k, :], w_hi[:, k, :].bitcast(F32), ALU.subtract
                ).then_inc(w_split, 1)

            def add_tile(T, t, parity, half):
                if half == 0:
                    dve.wait_ge(down_done, (T + 1) * CHUNKS)
                s = slice(half * SEQ, (half + 1) * SEQ)
                if isinstance(t, int):
                    a = acc[:, t, :, s]
                else:
                    a = acc[:, bass.ds(t, 1), :, s].rearrange("p a c n -> p (a c) n")
                c = T * HALVES + half
                c = coef[:, c : c + 1] if isinstance(c, int) else coef[:, bass.ds(c, 1)]
                ins = nc.vector.scalar_tensor_tensor(a, down_ps[:, parity, :, s], c, a, ALU.mult, ALU.add)
                if half == HALVES - 1:
                    ins.then_inc(tile_added, 1)

            def unit(T, k, first=False, between=None):
                n = T * CHUNKS + k
                dve.wait_ge(up_done, n + 1)
                dve.wait_ge(silu_done, n + 1)
                if not (first and k < S_BUFS):
                    dve.wait_ge(h_split, n + 1 - S_BUFS)
                nc.vector.tensor_tensor(
                    h[:, k % S_BUFS, :], silu[:, k % S_BUFS, :], up_ps[:, k % 2, :], ALU.mult
                ).then_inc(prod_done, 1)
                if between is not None:
                    between()
                dve.wait_ge(h_hi_done, n + 1)
                nc.vector.tensor_tensor(
                    h_lo[:, k % H_BUFS, :], h[:, k % S_BUFS, :], h_hi[:, k % H_BUFS, :].bitcast(F32), ALU.subtract
                ).then_inc(h_split, 1)

            def tile(T, parity, previous=None, first=False, splits=None):
                for k in range(CHUNKS):
                    between = None
                    if previous is not None and 1 <= k <= HALVES:
                        def between(half=k - 1):
                            add_tile(T - 1, previous, 1 - parity, half)
                    unit(T, k, first, between)
                    if splits is not None:
                        splits(k)

            def first_splits(k):
                if k + LEAD < CHUNKS:
                    split_weights(0, k + LEAD)

            def late_splits(e):
                return lambda k: split_weights(e, k + CHUNKS - FREED) if k < FREED else None

            def early_splits(e):
                return lambda k: split_weights(e, k - FREED) if k >= FREED else None

            def pairs_of(e):
                with dve.Fori(0, PAIRS) as q:
                    T = e * TILES + 2 * q + 1
                    tile(T, 1, previous=2 * q)
                    tile(T + 1, 0, previous=2 * q + 1)

            def coefficients():
                dve.wait_ge(gates_loaded, 32)
                nc.vector.tensor_scalar(routed_part[:], shared_sb[:], -1.0, 1.0, ALU.mult, ALU.add).then_inc(coef_steps, 1)
                nc.vector.tensor_copy(coef[:, ROUTED * BATCH :], shared_sb[:]).then_inc(coef_steps, 1)
                dve.wait_ge(coef_steps, 2)
                for e in range(ROUTED):
                    nc.vector.tensor_tensor(coef[:, e * BATCH : (e + 1) * BATCH], probs_sb[:, :, e], routed_part[:], ALU.mult).then_inc(coef_steps, 1)
                dve.wait_ge(coef_steps, 2 + ROUTED)

            last_t = TILES - 1
            nc.vector.memset(warm[:], 0.0).then_inc(warm_set, 1)
            dve.wait_ge(x0_loaded[0], 16)
            nc.vector.tensor_copy(x_hi[:, 0, 0, :], acc[:, 0, 0, :]).then_inc(x0_hi_done[0], 1)
            for c in range(DC):
                dve.wait_ge(x0_hi_done[c], 1)
                nc.vector.tensor_tensor(
                    x_lo[:, 0, c, :], acc[:, 0, c, :], x_hi[:, 0, c, :].bitcast(F32), ALU.subtract
                ).then_inc(x0_split, 1)
            dve.wait_ge(w0_gate_hi_done, 1)
            nc.vector.tensor_tensor(
                w_lo[:, 0, GATE], w_raw[:, 0, GATE], w_hi[:, 0, GATE].bitcast(F32), ALU.subtract
            ).then_inc(w0_gate_split, 1)
            dve.wait_ge(w_hi_done, 1)
            nc.vector.tensor_tensor(
                w_lo[:, 0, REST], w_raw[:, 0, REST], w_hi[:, 0, REST].bitcast(F32), ALU.subtract
            ).then_inc(w_split, 1)
            for k in range(1, LEAD):
                split_weights(0, k)
            tile(0, 0, first=True, splits=first_splits)
            coefficients()
            with dve.Fori(0, EXPERTS - 1) as e:
                pairs_of(e)
                T_last = e * TILES + last_t
                tile(T_last, 1, previous=last_t - 1, splits=early_splits(e + 1))
                tile(T_last + 1, 0, previous=last_t, splits=late_splits(e + 1))
            pairs_of(EXPERTS - 1)
            T_last = (EXPERTS - 1) * TILES + last_t
            tile(T_last, 1, previous=last_t - 1)
            for c in range(DC):
                if c < DC - 1:
                    dve.wait_ge(last_sums, c + 1)
                else:
                    dve.wait_ge(down_done, (T_last + 1) * CHUNKS)
                for half in range(HALVES):
                    s = slice(half * SEQ, (half + 1) * SEQ)
                    a, at = acc[:, last_t, c, s], T_last * HALVES + half
                    ins = nc.vector.scalar_tensor_tensor(
                        a, down_ps[:, 1, c, s], coef[:, at : at + 1], a, ALU.mult, ALU.add
                    )
                ins.then_inc(last_added, 1)


def kernel(x, fside_Bx8_0, condB_sharedgateprob, L0_cond_Wg, L0_cond_Wu, L0_cond_Wd, L0_cond_Sg, L0_cond_Su, L0_cond_Sd):
    import numpy as np
    import concourse.bacc as bacc
    from concourse.bass_utils import run_bass_kernel_spmd

    batch, seq, d = x.shape
    routed, _, f = L0_cond_Wg.shape
    tiles, dc, chunks = batch * seq // TOKENS, d // P, f // P

    xT = np.ascontiguousarray(np.asarray(x).reshape(tiles, TOKENS, dc, P).transpose(0, 3, 2, 1))

    def up(a):
        return a.reshape(-1, dc, P, chunks, P).transpose(0, 3, 2, 1, 4).reshape(-1, chunks, P, d)

    def down(a):
        return a.reshape(-1, chunks, P, d)

    w = np.concatenate(
        [
            np.concatenate([up(np.asarray(g)), up(np.asarray(u)), down(np.asarray(dn))], axis=3)
            for g, u, dn in ((L0_cond_Wg, L0_cond_Wu, L0_cond_Wd), (L0_cond_Sg, L0_cond_Su, L0_cond_Sd))
        ]
    )
    arrays = {
        "xT": xT,
        "w": np.ascontiguousarray(w),
        "probs": np.ascontiguousarray(fside_Bx8_0),
        "shared_gate": np.ascontiguousarray(condB_sharedgateprob),
    }
    nc = bacc.Bacc("TRN2", target_bir_lowering=False, num_devices=1)
    args = [nc.dram_tensor(n, a.shape, mybir.dt.from_np(a.dtype), kind="ExternalInput").ap() for n, a in arrays.items()]
    out = nc.dram_tensor("outT", xT.shape, F32, kind="ExternalOutput").ap()
    moe_kernel(nc, *args, out)
    r = run_bass_kernel_spmd(nc, [arrays], core_ids=[0])
    got = r.results[0]["outT"]
    return np.ascontiguousarray(got.transpose(0, 3, 2, 1)).reshape(batch, seq, d)
```
